# Optimizing a Trainium2 kernel written in Bass

```python
import numpy as np
import jax
import jax.numpy as jnp

def _softmax(x, axis=-1):
    return jax.nn.softmax(x, axis=axis)

def _gelu(x):
    return jax.nn.gelu(x, approximate=True)

def _silu(x):
    return jax.nn.silu(x)

def _sigmoid(x):
    return jax.nn.sigmoid(x)

def _layernorm(x, axis=-1, eps=1e-05):
    m = jnp.mean(x, axis=axis, keepdims=True)
    v = jnp.var(x, axis=axis, keepdims=True)
    return (x - m) / jnp.sqrt(v + eps)

def _scatter_add(tgt, idx, src, axis=0):
    return tgt.at[idx].add(src)

def _segment_sum(src, seg, n):
    return jax.ops.segment_sum(src, seg, n)
kernel_name = 'mk_seq_postln_d1_jaxref_r8_f91312'

def setup_inputs(seed: int=0):
    np.random.seed(seed)
    _w = jnp.asarray

    def _L0_attn_setup():
        import jax, jax.numpy as jnp
        import numpy as np
        import math
        E = 128
        B, T = (8, 256)
        key = jax.random.key(seed)
        ks = jax.random.split(key, 7)
        s = 1.0 / math.sqrt(E)
        return {'X': jax.random.normal(ks[0], (B, T, E), dtype=jnp.float32), 'Wq': jax.random.uniform(ks[1], (E, E), jnp.float32, -s, s), 'bq': jax.random.uniform(ks[2], (E,), jnp.float32, -s, s), 'Wk': jax.random.uniform(ks[3], (E, E), jnp.float32, -s, s), 'bk': jax.random.uniform(ks[4], (E,), jnp.float32, -s, s), 'Wv': jax.random.uniform(ks[5], (E, E), jnp.float32, -s, s), 'bv': jax.random.uniform(ks[6], (E,), jnp.float32, -s, s)}
    _L0_attn_in = _L0_attn_setup()

    def _L0_ffn_setup():
        import jax, jax.numpy as jnp
        import numpy as np
        B, S, H = (2, 128, 128)
        E, I, SI = (8, 64, 256)
        TOP_K, N_GROUP, TOPK_GROUP = (2, 2, 1)
        ROUTED_SCALE = 2.5

        def _route(x2d, gate_weight, gate_bias):
            T = x2d.shape[0]
            logits = x2d @ gate_weight.T
            scores = jax.nn.sigmoid(logits)
            sfc = scores + gate_bias[None, :]
            g = sfc.reshape(T, N_GROUP, E // N_GROUP)
            group_scores = jax.lax.top_k(g, 2)[0].sum(-1)
            _, gidx = jax.lax.top_k(group_scores, TOPK_GROUP)
            gmask = jnp.zeros((T, N_GROUP), sfc.dtype).at[jnp.arange(T)[:, None], gidx].set(1.0)
            smask = jnp.repeat(gmask, E // N_GROUP, axis=1)
            masked = jnp.where(smask > 0, sfc, 0.0)
            _, topk_idx = jax.lax.top_k(masked, TOP_K)
            topk_w = jnp.take_along_axis(scores, topk_idx, axis=1)
            topk_w = topk_w / (topk_w.sum(-1, keepdims=True) + 1e-20)
            topk_w = topk_w * ROUTED_SCALE
            return (topk_idx, topk_w)
        key = jax.random.key(seed)
        ks = jax.random.split(key, 7)

        def w(k, shape, sc=0.02):
            return jax.random.normal(k, shape, jnp.float32) * sc
        return {'hidden_states': jax.random.normal(ks[0], (B, S, H), jnp.float32), 'gate_weight': w(ks[1], (E, H)), 'gate_bias': w(ks[2], (E,), 0.01), 'up_weights': w(ks[3], (E, I, H)), 'down_weights': w(ks[4], (E, H, I)), 'shared_up_weight': w(ks[5], (SI, H)), 'shared_down_weight': w(ks[6], (H, SI))}
    _L0_ffn_in = _L0_ffn_setup()
    _d = {'L0_attn_X': _L0_attn_in['X'], 'L0_attn_Wq': _L0_attn_in['Wq'], 'L0_attn_bq': _L0_attn_in['bq'], 'L0_attn_Wk': _L0_attn_in['Wk'], 'L0_attn_bk': _L0_attn_in['bk'], 'L0_attn_Wv': _L0_attn_in['Wv'], 'L0_attn_bv': _L0_attn_in['bv'], 'L0_ffn_gate_weight': _L0_ffn_in['gate_weight'], 'L0_ffn_gate_bias': _L0_ffn_in['gate_bias'], 'L0_ffn_up_weights': _L0_ffn_in['up_weights'], 'L0_ffn_down_weights': _L0_ffn_in['down_weights'], 'L0_ffn_shared_up_weight': _L0_ffn_in['shared_up_weight'], 'L0_ffn_shared_down_weight': _L0_ffn_in['shared_down_weight']}
    _x0 = _d['L0_attn_X']
    _d['L0_attn_X'] = jax.random.normal(jax.random.fold_in(jax.random.key(seed), 1), (16, 512, 128), dtype=_x0.dtype)
    del _x0
    return _d

def reference(L0_attn_X, L0_attn_Wq, L0_attn_bq, L0_attn_Wk, L0_attn_bk, L0_attn_Wv, L0_attn_bv, L0_ffn_gate_weight, L0_ffn_gate_bias, L0_ffn_up_weights, L0_ffn_down_weights, L0_ffn_shared_up_weight, L0_ffn_shared_down_weight):

    def _L0_attn_ref(X, Wq, bq, Wk, bk, Wv, bv):
        import jax, jax.numpy as jnp
        import numpy as np
        import math
        E = 128
        B, T = (8, 256)
        q = jnp.einsum('bte,fe->btf', X, Wq) + bq
        k = jnp.einsum('bte,fe->btf', X, Wk) + bk
        v = jnp.einsum('bte,fe->btf', X, Wv) + bv
        scores = jnp.einsum('bie,bje->bij', q, k) / math.sqrt(E)
        i = jnp.arange(scores.shape[-2])[:, None]
        j = jnp.arange(scores.shape[-1])[None, :]
        scores = jnp.where(j > i, -jnp.inf, scores)
        attn = jax.nn.softmax(scores, axis=-2)
        return jnp.einsum('bij,bje->bie', attn, v)

    def _L0_ffn_ref(hidden_states, gate_weight, gate_bias, up_weights, down_weights, shared_up_weight, shared_down_weight):
        import jax, jax.numpy as jnp
        import numpy as np
        B, S, H = (2, 128, 128)
        E, I, SI = (8, 64, 256)
        TOP_K, N_GROUP, TOPK_GROUP = (2, 2, 1)
        ROUTED_SCALE = 2.5

        def _route(x2d, gate_weight, gate_bias):
            T = x2d.shape[0]
            logits = x2d @ gate_weight.T
            scores = jax.nn.sigmoid(logits)
            sfc = scores + gate_bias[None, :]
            g = sfc.reshape(T, N_GROUP, E // N_GROUP)
            group_scores = jax.lax.top_k(g, 2)[0].sum(-1)
            _, gidx = jax.lax.top_k(group_scores, TOPK_GROUP)
            gmask = jnp.zeros((T, N_GROUP), sfc.dtype).at[jnp.arange(T)[:, None], gidx].set(1.0)
            smask = jnp.repeat(gmask, E // N_GROUP, axis=1)
            masked = jnp.where(smask > 0, sfc, 0.0)
            _, topk_idx = jax.lax.top_k(masked, TOP_K)
            topk_w = jnp.take_along_axis(scores, topk_idx, axis=1)
            topk_w = topk_w / (topk_w.sum(-1, keepdims=True) + 1e-20)
            topk_w = topk_w * ROUTED_SCALE
            return (topk_idx, topk_w)
        Bv, Sv, Hv = hidden_states.shape
        x = hidden_states.reshape(-1, Hv)
        T = x.shape[0]
        topk_idx, topk_w = _route(x, gate_weight, gate_bias)
        cw = jnp.zeros((T, E), x.dtype).at[jnp.arange(T)[:, None], topk_idx].add(topk_w)
        h = jnp.einsum('th,eih->tei', x, up_weights)
        r = jnp.maximum(h, 0.0)
        r2 = r * r
        routed = jnp.einsum('tei,ehi,te->th', r2, down_weights, cw)
        sh = jnp.maximum(x @ shared_up_weight.T, 0.0)
        shared = sh * sh @ shared_down_weight.T
        return (routed + shared).reshape(Bv, Sv, Hv)
    x = L0_attn_X
    x = _layernorm(x + _L0_attn_ref(x, L0_attn_Wq, L0_attn_bq, L0_attn_Wk, L0_attn_bk, L0_attn_Wv, L0_attn_bv), axis=-1)
    x = _layernorm(x + _L0_ffn_ref(x, L0_ffn_gate_weight, L0_ffn_gate_bias, L0_ffn_up_weights, L0_ffn_down_weights, L0_ffn_shared_up_weight, L0_ffn_shared_down_weight), axis=-1)
    return x

_drawn_inputs = setup_inputs


def setup_inputs(seed=0):
    import zlib

    import numpy as np

    out = dict(_drawn_inputs(seed))
    spreads = {}
    factors = {'L0_attn_bq': 8.0,
     'L0_attn_bk': 8.0,
     'L0_ffn_gate_weight': 3.646,
     'L0_ffn_gate_bias': 8.0,
     'L0_ffn_up_weights': 3.507,
     'L0_ffn_down_weights': 3.175,
     'L0_ffn_shared_up_weight': 3.122,
     'L0_ffn_shared_down_weight': 2.832}
    for name, (base, spread) in spreads.items():
        noise = np.random.default_rng([zlib.crc32(name.encode()), seed]).standard_normal(out[name].shape)
        drawn = base * np.exp(spread * noise) if base else spread * noise
        out[name] = jnp.asarray(drawn.astype(out[name].dtype))
    for name, factor in factors.items():
        out[name] = (out[name] * factor).astype(out[name].dtype)
    return out
```

```python
from contextlib import ExitStack

import concourse.bass as bass
from concourse import mybir

ALU = mybir.AluOpType
ACT = mybir.ActivationFunctionType
AX = mybir.AxisListType
F32 = mybir.dt.float32
BF16 = mybir.dt.bfloat16

P = 128
EPS_LN = 1e-5
EPS_TOPK = 1e-20
ROUTED_SCALE = 2.5
MASKED = -1e30
SMALLEST = 1.17549435e-38


def layer_program(nc, X, XT, Wq, Wk, WvT, bq, bk, bv, gateT, gate_bias, up, down, out):
    SEQ, T, E = X.shape
    NT = T // P
    NB = up.shape[1]
    NX = gateT.shape[1]
    SH = NB - 4
    GROUP = NX // 2
    SCALE = float(E) ** -0.5
    S_AT = [sum(T - P * i for i in range(j)) for j in range(NT + 1)]

    with ExitStack() as ctx:
        def sb(name, shape, dt=F32):
            return ctx.enter_context(nc.sbuf_tensor(name, shape, dt))

        def pb(name, cols=512):
            return ctx.enter_context(nc.psum_tensor(name, [P, cols], F32))

        def sem(name):
            return ctx.enter_context(nc.semaphore(name))

        def row(vector):
            return vector.rearrange("(a n) -> a n", a=1)

        def column(vector):
            return vector.rearrange("(p a) -> p a", a=1)

        def tokens(tensor, k):
            return tensor[bass.ds(k, 1)].rearrange("a (t p) e -> p (a t) e", p=P)

        wq_sb, wk_sb = sb("wq_sb", [P, E]), sb("wk_sb", [P, E])
        wvr = sb("wvr", [P, E + 1])
        bq_sb, bk_sb = sb("bq_sb", [P, 1]), sb("bk_sb", [P, 1])
        bq_wide = sb("bq_wide", [P, P])
        bvr = sb("bvr", [P, E + 1])
        m_sb = sb("m_sb", [P, E])
        c_sb = sb("c_sb", [P, 1])
        gate_sb = sb("gate_sb", [P, NX])
        gbias = sb("gbias", [P, NX])
        up_sb = sb("up_sb", [P, NB, P])
        down_sb = sb("down_sb", [P, NB, E])
        ident = sb("ident", [P, P])
        ident16, mask16 = sb("ident16", [P, P], BF16), sb("mask16", [P, P], BF16)
        tie = sb("tie", [P, NX, NX])
        half, minus_half = sb("half", [P, NT * NX]), sb("minus_half", [P, NT])
        x_sb = [sb(f"x_sb{i}", [P, NT, E]) for i in range(2)]
        xT = [sb(f"xT{i}", [P, T]) for i in range(2)]
        wT = sb("wT", [P, T])
        v_sb = sb("v_sb", [P, NT, E + 1])
        vn = sb("vn", [P, NT, E])
        probsT = sb("probsT", [P, S_AT[NT]])
        neg_max, shift = sb("neg_max", [P, NT]), sb("shift", [P, NT])
        prob_sum, prob_inv = sb("prob_sum", [P, NT]), sb("prob_inv", [P, NT])
        y_sb = sb("y_sb", [P, NT, E])
        x1 = [sb(f"x1_{i}", [P, NT, E]) for i in range(2)]
        x1T = sb("x1T", [P, T])
        z_sb = sb("z_sb", [P, NT, E])
        z_out = [sb(f"z_out{i}", [P, NT, E]) for i in range(2)]
        stats = [sb(f"stats{i}", [P, NT, 6]) for i in range(2)]
        mean_var = [sb(f"mean_var{i}", [P, NT, 2]) for i in range(2)]
        neg_mean = [sb(f"neg_mean{i}", [P, NT]) for i in range(2)]
        var_eps = [sb(f"var_eps{i}", [P, NT]) for i in range(2)]
        rstd = [sb(f"rstd{i}", [P, NT]) for i in range(2)]
        exp_neg = sb("exp_neg", [P, NT, NX])
        one_plus = sb("one_plus", [P, NT, NX])
        score = sb("score", [P, NT, NX])
        biased = sb("biased", [P, NT, NX])
        pair_max, pair_min = sb("pair_max", [P, 2 * NT, 2]), sb("pair_min", [P, 2 * NT, 2])
        top1, low_max, high_min = sb("top1", [P, 2 * NT]), sb("low_max", [P, 2 * NT]), sb("high_min", [P, 2 * NT])
        top2 = sb("top2", [P, 2 * NT])
        group_score = sb("group_score", [P, NT, 2])
        group_mask = sb("group_mask", [P, NT, 2])
        masked = sb("masked", [P, NT, NX])
        diff = sb("diff", [P, NT, NX, NX])
        ahead = sb("ahead", [P, NT, NX, NX])
        rank = sb("rank", [P, NT, NX])
        chosen = sb("chosen", [P, NT, NX])
        weight_sum, weight_den, weight_inv = sb("weight_sum", [P, NT]), sb("weight_den", [P, NT]), sb("weight_inv", [P, NT])
        weight = sb("weight", [P, NT, NX])
        root = sb("root", [P, NT, NX])
        root_wide = sb("root_wide", [P, NT, NX, P // NX])
        rootT = sb("rootT", [P, T])
        g_sb = [sb(f"g_sb{i}", [P, T]) for i in range(2)]
        r2 = [sb(f"r2_{i}", [P, T]) for i in range(3)]

        bank_a, bank_b = pb("bank_a"), pb("bank_b")
        bank_s = [pb("bank_s0"), pb("bank_s1")]
        bank_o, bank_y = pb("bank_o"), pb("bank_y")
        bank_h = [pb("bank_h0"), pb("bank_h1")]

        weights_in = sem("weights_in")
        x_in = [sem(f"x_in{i}") for i in range(2)]
        xT_in = [sem(f"xT_in{i}") for i in range(2)]
        stored = [sem(f"stored{i}") for i in range(2)]
        pool_const, bq_spread, setup_made, setup_kept = sem("pool_const"), sem("bq_spread"), sem("setup_made"), sem("setup_kept")
        w_made, w_kept = sem("w_made"), sem("w_kept")
        v_made, v_kept, v_scaled = sem("v_made"), sem("v_kept"), sem("v_scaled")
        s_made, max_set, shift_set = sem("s_made"), sem("max_set"), sem("shift_set")
        exp_done, inv_set, o_made = sem("exp_done"), sem("inv_set"), sem("o_made")
        y_set, y_bn = sem("y_set"), sem("y_bn")
        y_stats, y_scale, x1_set = sem("y_stats"), sem("y_scale"), sem("x1_set")
        x1T_made, x1T_kept = sem("x1T_made"), sem("x1T_kept")
        logits_made, exp_neg_set = sem("logits_made"), sem("exp_neg_set")
        route, weight_set = sem("route"), sem("weight_set")
        root_set, root_spread = sem("root_set"), sem("root_spread")
        rootT_made, rootT_kept = sem("rootT_made"), sem("rootT_kept")
        h_made, g_set, r2_set, down_done = sem("h_made"), sem("g_set"), sem("r2_set"), sem("down_done")
        z_sum, z_bn = sem("z_sum"), sem("z_bn")
        z_stats, z_scale, z_set = sem("z_stats"), sem("z_scale"), sem("z_set")
        ROUTE = 16

        def after(eng, signal, per, k, n):
            count = k * per + n
            if not isinstance(count, int) or count > 0:
                eng.wait_ge(signal, count)

        def after_alone(eng, signal, per, k, n):
            count = k * per + n
            if not isinstance(count, int):
                count = eng.lower_val(count)
            if not isinstance(count, int) or count > 0:
                eng.wait_ge(pool_const, 9)
                eng.wait_ge(signal, count)

        def run(eng, step):
            step(0, 0, 0, experts=False)
            step(1, 1, 0)
            with eng.Fori(1, SEQ // 2) as turn:
                step(turn * 2, 0, turn)
                step(turn * 2 + 1, 1, turn)
            step(SEQ, 0, SEQ // 2, attention=False)

        block = ctx.enter_context(nc.Block())

        @block.sync
        def _(sp):
            sp.dma_start(wq_sb[:], Wq).then_inc(weights_in, 16)
            sp.dma_start(wk_sb[:], Wk).then_inc(weights_in, 16)
            sp.dma_start(bq_sb[:], column(bq)).then_inc(weights_in, 16)
            sp.dma_start(bk_sb[:], column(bk)).then_inc(weights_in, 16)
            sp.dma_start(xT[0][:], XT[0]).then_inc(xT_in[0], 16)
            sp.dma_start(wvr[:, 0:E], WvT).then_inc(weights_in, 16)
            sp.dma_start(bvr[:, 0:E], row(bv).to_broadcast([P, E])).then_inc(weights_in, 16)
            sp.dma_start(x_sb[0][:], tokens(X, 0)).then_inc(x_in[0], 16)
            sp.dma_start(gate_sb[:], gateT).then_inc(weights_in, 16)
            sp.dma_start(gbias[:], row(gate_bias).to_broadcast([P, NX])).then_inc(weights_in, 16)
            sp.dma_start(up_sb[:], up).then_inc(weights_in, 16)
            sp.dma_start(down_sb[:], down).then_inc(weights_in, 16)
            sp.dma_start(xT[1][:], XT[1]).then_inc(xT_in[1], 16)
            sp.dma_start(x_sb[1][:], tokens(X, 1)).then_inc(x_in[1], 16)

            def load(k, par):
                after(sp, s_made, NT, k - 2, NT)
                sp.dma_start(xT[par][:], XT[bass.ds(k, 1)].rearrange("a p t -> (a p) t")).then_inc(xT_in[par], 16)
                after(sp, y_set, 1, k - 2, 1)
                sp.dma_start(x_sb[par][:], tokens(X, k)).then_inc(x_in[par], 16)

            def store(k, par):
                after(sp, z_set, 1, k, 1)
                sp.dma_start(tokens(out, k), z_out[par][:]).then_inc(stored[par], 16)

            with sp.Fori(1, SEQ // 2) as turn:
                load(turn * 2, 0)
                store(turn * 2 - 2, 0)
                load(turn * 2 + 1, 1)
                store(turn * 2 - 1, 1)
            store(SEQ - 2, 0)
            store(SEQ - 1, 1)
            for par in range(2):
                sp.wait_ge(stored[par], 16 * (SEQ // 2))

        @block.gpsimd
        def _(pool):
            pool.memset(ident[:], 0.0).then_inc(pool_const, 1)
            pool.memset(mask16[:], 0.0).then_inc(pool_const, 1)
            pool.memset(tie[:], SMALLEST).then_inc(pool_const, 1)
            pool.memset(half[:], 0.5).then_inc(pool_const, 1)
            pool.memset(minus_half[:], -0.5).then_inc(pool_const, 1)
            pool.wait_ge(pool_const, 5)
            pool.affine_select(out=ident[:], in_=ident[:], compare_op=ALU.not_equal, fill=1.0, base=0,
                               pattern=[[-1, P]], channel_multiplier=1).then_inc(pool_const, 1)
            pool.affine_select(out=mask16[:], in_=mask16[:], compare_op=ALU.is_ge, fill=MASKED, base=0,
                               pattern=[[1, P]], channel_multiplier=-1).then_inc(pool_const, 1)
            pool.affine_select(out=tie[:], in_=tie[:], compare_op=ALU.is_ge, fill=0.0, base=0,
                               pattern=[[-1, NX], [1, NX]], channel_multiplier=0).then_inc(pool_const, 1)
            pool.wait_ge(pool_const, 8)
            pool.tensor_copy(ident16[:], ident[:]).then_inc(pool_const, 1)

            def normalise(k, n, src, dst, scale_set, done):
                pool.tensor_scalar(neg_mean[n][:], mean_var[n][:, :, 0], -1.0, 0.0, ALU.mult, ALU.add)
                pool.tensor_scalar(var_eps[n][:], mean_var[n][:, :, 1], 1.0, EPS_LN, ALU.mult, ALU.add)\
                    .then_inc(scale_set, 1)
                after(pool, scale_set, 2, k, 1)
                pool.tensor_tensor(rstd[n][:], var_eps[n][:], minus_half[:], ALU.pow).then_inc(scale_set, 1)
                after_alone(pool, scale_set, 2, k, 2)
                for t in range(NT):
                    last = pool.tensor_scalar(dst[:, t, :], src[:, t, :], neg_mean[n][:, t:t + 1],
                                              rstd[n][:, t:t + 1], ALU.add, ALU.mult)
                last.then_inc(done, 1)

            def step(k, par, half_k, attention=True, experts=True):
                m, m_par = k - 1, 1 - par
                m_half = half_k - 1 + par
                if experts:
                    after(pool, weight_set, 1, m, 1)
                    after(pool, rootT_made, 1, m, 0)
                    pool.tensor_tensor(root[:], weight[:], half[:].rearrange("p (t e) -> p t e", e=NX), ALU.pow)\
                        .then_inc(root_set, 1)
                    after_alone(pool, root_set, 1, m, 1)
                    pool.tensor_copy(root_wide[:], root[:].unsqueeze(3).to_broadcast([P, NT, NX, P // NX]))\
                        .then_inc(root_spread, 1)
                if attention:
                    after(pool, inv_set, 1, k, 1)
                    after(pool, v_kept, 2, k, 2)
                    after(pool, o_made, 1, k, 0)
                    pool.tensor_tensor(vn[:], v_sb[:, :, 0:E], prob_inv[:].unsqueeze(2).to_broadcast([P, NT, E]), ALU.mult)\
                        .then_inc(v_scaled, 1)
                    after_alone(pool, y_stats, 1, k, 1)
                    after_alone(pool, z_sum, 1, k - 2, 1)
                    normalise(k, 0, y_sb, x1[par], y_scale, x1_set)
                if experts:
                    after_alone(pool, z_stats, 1, m, 1)
                    after_alone(pool, stored[m_par], 16, m_half, 0)
                    normalise(m, 1, z_sb, z_out[m_par], z_scale, z_set)

            run(pool, step)

        @block.scalar
        def _(act):
            act.wait_ge(setup_made, 1)
            act.mul(m_sb[:], bank_a[:, 0:E], SCALE)
            act.mul(c_sb[:], bank_a[:, E:E + 1], SCALE)
            act.mul(wvr[:, E:E + 1], bank_a[:, E + 1:E + 2], SCALE)
            act.mul(bvr[:, E:E + 1], bank_a[:, E + 2:E + 3], SCALE).then_inc(setup_kept, 1)
            act.wait_ge(setup_kept, 1)

            def step(k, par, half_k, attention=True, experts=True):
                m = k - 1

                def exponentials(j):
                    n = T - P * j
                    after(act, shift_set, NT, k, j + 1)
                    after(act, o_made, 1, k, 0)
                    act.activation(probsT[:, S_AT[j]:S_AT[j] + n], bank_s[j % 2][:, 0:n], ACT.Exp,
                                   bias=shift[:, j:j + 1], accum_out=prob_sum[:, j:j + 1]).then_inc(exp_done, 1)

                def square(b):
                    after(act, g_set, NB, m, b + 1)
                    after(act, down_done, NB, m, b - 2)
                    act.activation(r2[b % 3][:], g_sb[b % 2][:], ACT.Square).then_inc(r2_set, 1)

                if experts:
                    after(act, logits_made, 1, m, 1)
                    after(act, weight_set, 1, m, 0)
                    act.activation(exp_neg[:], bank_a[:, 0:NT * NX].rearrange("p (t e) -> p t e", e=NX), ACT.Exp,
                                   scale=-1.0).then_inc(exp_neg_set, 1)
                if attention:
                    after(act, w_made, 1, k, 1)
                    act.activation(wT[:], bank_a[:], ACT.Identity, bias=c_sb[:, 0:1]).then_inc(w_kept, 1)
                if experts:
                    square(0)
                    square(1)
                if attention:
                    exponentials(0)
                    exponentials(1)
                if experts:
                    after(act, rootT_made, 1, m, 1)
                    after(act, g_set, NB, m, 0)
                    act.copy(rootT[:], bank_b[:]).then_inc(rootT_kept, 1)
                if attention:
                    exponentials(2)
                    exponentials(3)
                if experts:
                    for b in range(2, NB):
                        square(b)
                if attention:
                    after(act, x1T_made, 1, k, 1)
                    act.copy(x1T[:], bank_b[:]).then_inc(x1T_kept, 1)

            run(act, step)

        @block.vector
        def _(dve):
            dve.wait_ge(weights_in, 16 * 10)
            dve.tensor_copy(bq_wide[:], bq_sb[:, 0:1].to_broadcast([P, P])).then_inc(bq_spread, 1)
            dve.wait_ge(setup_kept, 1)
            dve.wait_ge(pool_const, 9)

            def router(m):
                links = [0]

                def link(instruction):
                    links[0] += 1
                    instruction.then_inc(route, 1)
                    after(dve, route, ROUTE, m, links[0])

                after(dve, exp_neg_set, 1, m, 1)
                link(dve.tensor_scalar(one_plus[:], exp_neg[:], 1.0, None, ALU.add))
                link(dve.reciprocal(score[:], one_plus[:]))
                link(dve.tensor_tensor(biased[:], score[:], gbias[:].unsqueeze(1).to_broadcast([P, NT, NX]), ALU.add))
                fours = biased[:].rearrange("p t (g i) -> p (t g) i", i=GROUP)
                dve.tensor_tensor(pair_max[:], fours[:, :, 0:2], fours[:, :, 2:4], ALU.max)
                link(dve.tensor_tensor(pair_min[:], fours[:, :, 0:2], fours[:, :, 2:4], ALU.min))
                dve.tensor_tensor(top1[:], pair_max[:, :, 0], pair_max[:, :, 1], ALU.max)
                dve.tensor_tensor(low_max[:], pair_max[:, :, 0], pair_max[:, :, 1], ALU.min)
                link(dve.tensor_tensor(high_min[:], pair_min[:, :, 0], pair_min[:, :, 1], ALU.max))
                link(dve.tensor_tensor(top2[:], low_max[:], high_min[:], ALU.max))
                link(dve.tensor_tensor(group_score[:].rearrange("p t g -> p (t g)"), top1[:], top2[:], ALU.add))
                dve.tensor_tensor(group_mask[:, :, 0], group_score[:, :, 0], group_score[:, :, 1], ALU.is_ge)
                link(dve.tensor_tensor(group_mask[:, :, 1], group_score[:, :, 0], group_score[:, :, 1], ALU.is_lt))
                link(dve.tensor_tensor(masked[:].rearrange("p t (g i) -> p (t g) i", i=GROUP), fours,
                                       group_mask[:].rearrange("p t g -> p (t g)").unsqueeze(2).to_broadcast([P, 2 * NT, GROUP]),
                                       ALU.mult))
                link(dve.tensor_tensor(diff[:], masked[:].unsqueeze(2).to_broadcast([P, NT, NX, NX]),
                                       masked[:].unsqueeze(3).to_broadcast([P, NT, NX, NX]), ALU.subtract))
                link(dve.tensor_tensor(ahead[:].rearrange("p t e j -> p t (e j)"), diff[:].rearrange("p t e j -> p t (e j)"),
                                       tie[:].rearrange("p e j -> p (e j)").unsqueeze(1).to_broadcast([P, NT, NX * NX]), ALU.is_ge))
                link(dve.tensor_reduce(rank[:], ahead[:], AX.X, ALU.add))
                link(dve.scalar_tensor_tensor(out=chosen[:], in0=rank[:], scalar=2.0, in1=score[:], op0=ALU.is_lt, op1=ALU.mult))
                link(dve.tensor_reduce(weight_sum[:], chosen[:], AX.X, ALU.add))
                link(dve.tensor_scalar(weight_den[:], weight_sum[:], EPS_TOPK, 1.0 / ROUTED_SCALE, ALU.add, ALU.mult))
                link(dve.reciprocal(weight_inv[:], weight_den[:]))
                after(dve, root_set, 1, m, 0)
                dve.tensor_tensor(weight[:], chosen[:], weight_inv[:].unsqueeze(2).to_broadcast([P, NT, NX]), ALU.mult)\
                    .then_inc(weight_set, 1)
                assert links[0] == ROUTE

            def step(k, par, half_k, attention=True, experts=True):
                m, m_par = k - 1, 1 - par

                def gated(b):
                    after(dve, h_made, NB, m, b + 1)
                    after(dve, r2_set, NB, m, b - 1)
                    if b < SH:
                        dve.tensor_scalar(g_sb[b % 2][:], bank_h[b % 2][:], 0.0, None, ALU.max).then_inc(g_set, 1)
                    else:
                        after(dve, rootT_kept, 1, m, 1)
                        dve.scalar_tensor_tensor(out=g_sb[b % 2][:], in0=bank_h[b % 2][:], scalar=0.0, in1=rootT[:],
                                                 op0=ALU.max, op1=ALU.mult).then_inc(g_set, 1)

                def values(n, bank):
                    after(dve, v_made, 2, k, n + 1)
                    after(dve, v_scaled, 1, k, 0)
                    dve.tensor_tensor(v_sb[:, 2 * n:2 * n + 2, :], bank[:, 0:2 * (E + 1)].rearrange("p (t e) -> p t e", t=2),
                                      bvr[:].unsqueeze(1).to_broadcast([P, 2, E + 1]), ALU.add).then_inc(v_kept, 1)

                def key_shift(j):
                    after(dve, s_made, NT, k, j + 1)
                    dve.reduce_max(neg_max[:, j:j + 1], bank_s[j % 2][:, 0:T - P * j], AX.X, negate=True).then_inc(max_set, 1)
                    after(dve, max_set, NT, k, j + 1)
                    after(dve, v_kept, 2, k, j // 2 + 1)
                    dve.tensor_scalar(shift[:, j:j + 1], neg_max[:, j:j + 1], v_sb[:, j, E:E + 1], v_sb[:, j, E:E + 1],
                                      ALU.subtract, ALU.add).then_inc(shift_set, 1)

                def token_stats(seq, src, n, bn, done):
                    for t in range(NT):
                        last = dve.bn_stats(stats[n][:, t, :], src[:, t, :])
                    last.then_inc(bn, 1)
                    after_alone(dve, bn, 1, seq, 1)
                    for t in range(NT):
                        last = dve.bn_aggr(mean_var[n][:, t, :], stats[n][:, t, :])
                    last.then_inc(done, 1)

                if experts:
                    router(m)
                    gated(0)
                    gated(1)
                if attention:
                    values(0, bank_b)
                    key_shift(0)
                    key_shift(1)
                    values(1, bank_a)
                    key_shift(2)
                    key_shift(3)
                if experts:
                    gated(2)
                    gated(3)
                if attention:
                    after(dve, exp_done, NT, k, NT)
                    dve.reciprocal(prob_inv[:], prob_sum[:]).then_inc(inv_set, 1)
                if experts:
                    gated(4)
                if attention:
                    after(dve, o_made, 1, k, 1)
                    after(dve, x_in[par], 16, half_k, 16)
                    after(dve, x1_set, 1, k, 0)
                    dve.tensor_tensor(y_sb[:].rearrange("p t e -> p (t e)"), bank_o[:],
                                      x_sb[par][:].rearrange("p t e -> p (t e)"), ALU.add).then_inc(y_set, 1)
                    after(dve, y_set, 1, k, 1)
                    token_stats(k, y_sb, 0, y_bn, y_stats)
                if experts:
                    gated(5)
                    after(dve, down_done, NB, m, NB)
                    after(dve, z_set, 1, m, 0)
                    dve.tensor_tensor(z_sb[:].rearrange("p t e -> p (t e)"), bank_y[:],
                                      x1[m_par][:].rearrange("p t e -> p (t e)"), ALU.add).then_inc(z_sum, 1)
                    after(dve, z_sum, 1, m, 1)
                    token_stats(m, z_sb, 1, z_bn, z_stats)

            run(dve, step)

        @block.tensor
        def _(pe):
            pe.wait_ge(weights_in, 16 * 10)
            pe.wait_ge(bq_spread, 1)
            pe.matmul(bank_a[:, 0:E], wk_sb[:], wq_sb[:], start=True, stop=True)
            pe.matmul(bank_a[:, E:E + 1], wq_sb[:], bk_sb[:], start=True, stop=True)
            pe.matmul(bank_a[:, E + 1:E + 2], wk_sb[:], bq_sb[:], start=True, stop=True)
            pe.matmul(bank_a[:, E + 2:E + 3], bq_wide[:], bk_sb[:], start=True, stop=True).then_inc(setup_made, 1)
            pe.wait_ge(setup_kept, 1)
            pe.wait_ge(pool_const, 9)

            def step(k, par, half_k, attention=True, experts=True):
                m = k - 1

                def up_block(b):
                    after(pe, x1T_kept, 1, m, 1)
                    after(pe, g_set, NB, m, b - 1)
                    pe.matmul(bank_h[b % 2][:], up_sb[:, b, :], x1T[:], start=True, stop=True).then_inc(h_made, 1)

                def down_block(b):
                    after(pe, r2_set, NB, m, b + 1)
                    after(pe, z_sum, 1, m, 0)
                    for t in range(NT):
                        last = pe.matmul(bank_y[:, t * E:(t + 1) * E], r2[b % 3][:, t * P:(t + 1) * P], down_sb[:, b, :],
                                         start=(b == 0 and t == 0), stop=(b == NB - 1), skip_group_check=True)
                    last.then_inc(down_done, 1)

                def values(n, bank):
                    for t in range(2):
                        tile = 2 * n + t
                        last = pe.matmul(bank[:, t * (E + 1):(t + 1) * (E + 1)], xT[par][:, tile * P:(tile + 1) * P], wvr[:],
                                         start=True, stop=True)
                    last.then_inc(v_made, 1)

                def scores(j):
                    n = T - P * j
                    after(pe, exp_done, NT, k, j - 1)
                    pe.matmul(bank_s[j % 2][:, 0:n], wT[:, j * P:(j + 1) * P], xT[par][:, j * P:T], start=True, stop=False,
                              skip_group_check=True)
                    pe.matmul(bank_s[j % 2][:, 0:P], ident16[:], mask16[:], start=False, stop=True,
                              skip_group_check=True).then_inc(s_made, 1)

                if attention:
                    after(pe, xT_in[par], 16, half_k, 16)
                    after(pe, exp_neg_set, 1, k, 0)
                    pe.matmul(bank_a[:], m_sb[:], xT[par][:], start=True, stop=True).then_inc(w_made, 1)
                if experts:
                    up_block(0)
                    up_block(1)
                if attention:
                    after(pe, x1T_kept, 1, k, 0)
                    values(0, bank_b)
                    after(pe, w_kept, 1, k, 1)
                    scores(0)
                    scores(1)
                    values(1, bank_a)
                if experts:
                    after(pe, root_spread, 1, m, 1)
                    if attention:
                        after(pe, v_kept, 2, k, 1)
                    else:
                        after(pe, x1T_kept, 1, m, 1)
                    for t in range(NT):
                        last = pe.transpose(bank_b[:, t * P:(t + 1) * P], root_wide[:, t].rearrange("p e c -> p (e c)"), ident[:])
                    last.then_inc(rootT_made, 1)
                    down_block(0)
                    down_block(1)
                if attention:
                    scores(2)
                    scores(3)
                if experts:
                    up_block(2)
                    up_block(3)
                if attention:
                    after(pe, v_scaled, 1, k, 1)
                    after(pe, exp_done, NT, k, NT)
                    after(pe, y_set, 1, k, 0)
                    for t in range(NT):
                        for j in range(t + 1):
                            at = S_AT[j] + (t - j) * P
                            last = pe.matmul(bank_o[:, t * E:(t + 1) * E], probsT[:, at:at + P], vn[:, j, :],
                                             start=(j == 0), stop=(j == t))
                    last.then_inc(o_made, 1)
                if experts:
                    down_block(2)
                    up_block(4)
                    down_block(3)
                    up_block(5)
                    down_block(4)
                    down_block(5)
                if attention:
                    after(pe, x1_set, 1, k, 1)
                    if experts:
                        after(pe, rootT_kept, 1, m, 1)
                    else:
                        after(pe, v_kept, 2, k, 1)
                    for t in range(NT):
                        last = pe.transpose(bank_b[:, t * P:(t + 1) * P], x1[par][:, t, :], ident[:])
                    last.then_inc(x1T_made, 1)
                    after(pe, x1T_kept, 1, k, 1)
                    after(pe, v_kept, 2, k, 2)
                    for t in range(NT):
                        last = pe.matmul(bank_a[:, t * NX:(t + 1) * NX], x1T[:, t * P:(t + 1) * P], gate_sb[:],
                                         start=True, stop=True)
                    last.then_inc(logits_made, 1)

            run(pe, step)


def kernel(**inputs):
    import numpy as np
    import concourse.bacc as bacc
    from concourse.bass_utils import run_bass_kernel_spmd

    a = {name: np.asarray(value) for name, value in inputs.items()}
    X = a["L0_attn_X"]
    seq, t, e = X.shape
    routed_up, routed_down = a["L0_ffn_up_weights"], a["L0_ffn_down_weights"]
    nx, width, h = routed_up.shape
    share = P // nx
    shared_up, shared_down = a["L0_ffn_shared_up_weight"], a["L0_ffn_shared_down_weight"]
    up = np.concatenate([
        shared_up.reshape(-1, P, h).transpose(2, 0, 1),
        routed_up.reshape(nx, width // share, share, h).transpose(3, 1, 0, 2).reshape(h, width // share, P)], 1)
    down = np.concatenate([
        shared_down.reshape(h, -1, P).transpose(2, 1, 0),
        routed_down.reshape(nx, h, width // share, share).transpose(0, 3, 2, 1).reshape(P, width // share, h)], 1)
    arrays = {
        "X": X, "XT": X.transpose(0, 2, 1), "Wq": a["L0_attn_Wq"], "Wk": a["L0_attn_Wk"], "WvT": a["L0_attn_Wv"].T,
        "bq": a["L0_attn_bq"], "bk": a["L0_attn_bk"], "bv": a["L0_attn_bv"], "gateT": a["L0_ffn_gate_weight"].T,
        "gate_bias": a["L0_ffn_gate_bias"], "up": up, "down": down,
    }
    arrays = {name: np.ascontiguousarray(value) for name, value in arrays.items()}
    nc = bacc.Bacc("TRN2", target_bir_lowering=False, num_devices=1)
    args = {name: nc.dram_tensor(name, value.shape, F32, kind="ExternalInput").ap() for name, value in arrays.items()}
    args["out"] = nc.dram_tensor("out", X.shape, F32, kind="ExternalOutput").ap()
    layer_program(nc, **args)
    return run_bass_kernel_spmd(nc, [arrays], core_ids=[0]).results[0]["out"]
```

```python
from contextlib import ExitStack

import concourse.bass as bass
from concourse import mybir

ALU = mybir.AluOpType
ACT = mybir.ActivationFunctionType
AX = mybir.AxisListType
F32 = mybir.dt.float32
BF16 = mybir.dt.bfloat16
F16 = mybir.dt.float16
I32 = mybir.dt.int32

P = 128
EPS_LN = 1e-5
EPS_TOPK = 1e-20
ROUTED_SCALE = 2.5
MASKED = -1e30
SMALLEST = 1.17549435e-38
EXPONENT_BITS = 0x7F800000
WEIGHT_FLOOR = 1e-18
UNIT_FLOOR = 1e-30
RMAX = bass.bass_isa.ReduceOp.max
HI, LO = 0, 1


def layer_program(nc, X, XT, Wq, Wk, WvT, bq, bk, bv, gateT, gate_bias, up, down, out):
    SEQ, T, E = X.shape
    NT = T // P
    NB = up.shape[1]
    NX = gateT.shape[1]
    SH = NB - 4
    GROUP = NX // 2
    SCALE = float(E) ** -0.5
    S_AT = [sum(T - P * i for i in range(j)) for j in range(NT + 1)]

    with ExitStack() as ctx:
        def sb(name, shape, dt=F32):
            return ctx.enter_context(nc.sbuf_tensor(name, shape, dt))

        def pb(name, cols=512):
            return ctx.enter_context(nc.psum_tensor(name, [P, cols], F32))

        def sem(name):
            return ctx.enter_context(nc.semaphore(name))

        def row(vector):
            return vector.rearrange("(a n) -> a n", a=1)

        def column(vector):
            return vector.rearrange("(p a) -> p a", a=1)

        def tokens(tensor, k):
            return tensor[bass.ds(k, 1)].rearrange("a (t p) e -> p (a t) e", p=P)

        wq_sb, wk_sb = sb("wq_sb", [P, E]), sb("wk_sb", [P, E])
        wvr = sb("wvr", [P, E + 1])
        bq_sb, bk_sb = sb("bq_sb", [P, 1]), sb("bk_sb", [P, 1])
        bq_wide = sb("bq_wide", [P, P])
        bvr = sb("bvr", [P, E + 1])
        m_sb = sb("m_sb", [P, E])
        c_sb = sb("c_sb", [P, 1])
        gate_sb = sb("gate_sb", [P, NX])
        gbias = sb("gbias", [P, NX])
        up_sb = sb("up_sb", [P, NB, P])
        down_sb = sb("down_sb", [P, NB, E])
        gate_parts = sb("gate_parts", [P, 2, NX], F16)
        up_parts = sb("up_parts", [P, 2, NB, P], F16)
        down_parts = sb("down_parts", [P, 2, NB, E], F16)
        largest, largest_all = sb("largest", [P, 3]), sb("largest_all", [P, 3])
        floor2, over2 = sb("floor2", [P, 3]), sb("over2", [P, 3])
        neg_gate_unit, up_unit2, ffn_unit = sb("neg_gate_unit", [P, 1]), sb("up_unit2", [P, 1]), sb("ffn_unit", [P, 1])
        ident = sb("ident", [P, P])
        ident16, mask16 = sb("ident16", [P, P], BF16), sb("mask16", [P, P], BF16)
        ident_half = sb("ident_half", [P, P], F16)
        tie = sb("tie", [P, NX, NX])
        minus_half, eps_ln = sb("minus_half", [P, NT]), sb("eps_ln", [P, NT])
        weight_floor = sb("weight_floor", [P, 1])
        x_sb = [sb(f"x_sb{i}", [P, NT, E]) for i in range(2)]
        xT = [sb(f"xT{i}", [P, T]) for i in range(2)]
        wT = sb("wT", [P, T])
        v_sb = sb("v_sb", [P, NT, E + 1])
        vn = sb("vn", [P, NT, E])
        probsT = sb("probsT", [P, S_AT[NT]])
        neg_max, shift = sb("neg_max", [P, NT]), sb("shift", [P, NT])
        prob_sum, prob_inv = sb("prob_sum", [P, NT]), sb("prob_inv", [P, NT])
        y_sb = sb("y_sb", [P, NT, E])
        x1 = [sb(f"x1_{i}", [P, NT, E]) for i in range(4)]
        x1_parts = sb("x1_parts", [P, 2, NT, E], F16)
        x1T = [sb(f"x1T{i}", [P, 2, T], F16) for i in range(2)]
        z_sb = sb("z_sb", [P, NT, E])
        z_out = [sb(f"z_out{i}", [P, NT, E]) for i in range(2)]
        stats = [sb(f"stats{i}", [P, NT, 6]) for i in range(2)]
        mean_var = [sb(f"mean_var{i}", [P, NT, 2]) for i in range(2)]
        var_eps = [sb(f"var_eps{i}", [P, NT]) for i in range(2)]
        rstd = [sb(f"rstd{i}", [P, NT]) for i in range(2)]
        exp_neg = sb("exp_neg", [P, NT, NX])
        one_plus = sb("one_plus", [P, NT, NX])
        score = sb("score", [P, NT, NX])
        biased = sb("biased", [P, NT, NX])
        pair_sum = sb("pair_sum", [P, 2 * NT, 6])
        group_score = sb("group_score", [P, NT, 2])
        group_mask = sb("group_mask", [P, NT, 2])
        masked = sb("masked", [P, NT, NX])
        diff = sb("diff", [P, NT, NX, NX])
        ahead = sb("ahead", [P, NT, NX, NX])
        rank = sb("rank", [P, NT, NX])
        chosen = sb("chosen", [P, NT, NX])
        weight_sum, weight_den, weight_inv = sb("weight_sum", [P, NT]), sb("weight_den", [P, NT]), sb("weight_inv", [P, NT])
        weight = sb("weight", [P, NT, NX])
        log_weight, root_guess = sb("log_weight", [P, NT, NX]), sb("root_guess", [P, NT, NX])
        guess2, newton = sb("guess2", [P, NT, NX]), sb("newton", [P, NT, NX])
        guess_weight = sb("guess_weight", [P, NT, NX])
        root, root_wide = sb("root", [P, NT, NX]), sb("root_wide", [P, NT * NX, P // NX])
        rootT = sb("rootT", [P, T])
        g_sb = [sb(f"g_sb{i}", [P, T]) for i in range(2)]
        r2_sb = [sb(f"r2_sb{i}", [P, T]) for i in range(2)]
        r2 = [sb(f"r2_{i}", [P, 2, T], F16) for i in range(3)]

        bank_a, bank_b = pb("bank_a"), pb("bank_b")
        bank_s = [pb("bank_s0"), pb("bank_s1")]
        bank_o, bank_y = pb("bank_o"), pb("bank_y")
        bank_h = [pb("bank_h0"), pb("bank_h1")]

        scores_in, values_in, experts_in = sem("scores_in"), sem("values_in"), sem("experts_in")
        x_in = [sem(f"x_in{i}") for i in range(2)]
        xT_in = [sem(f"xT_in{i}") for i in range(2)]
        stored = [sem(f"stored{i}") for i in range(2)]
        parts_set, parts_hi, largest_set = sem("parts_set"), sem("parts_hi"), sem("largest_set")
        pool_const, bq_spread, setup_made, setup_kept = sem("pool_const"), sem("bq_spread"), sem("setup_made"), sem("setup_kept")
        w_made, w_kept = sem("w_made"), sem("w_kept")
        v_made, v_kept, v_scaled = sem("v_made"), sem("v_kept"), sem("v_scaled")
        s_made, max_set, shift_set = sem("s_made"), sem("max_set"), sem("shift_set")
        exp_done, inv_set, o_made = sem("exp_done"), sem("inv_set"), sem("o_made")
        y_set, y_bn = sem("y_set"), sem("y_bn")
        y_stats, y_scale, x1_set = sem("y_stats"), sem("y_scale"), sem("x1_set")
        x1_hi, x1_lo = sem("x1_hi"), sem("x1_lo")
        x1T_made, x1T_kept = sem("x1T_made"), sem("x1T_kept")
        logits_made, exp_neg_set = sem("logits_made"), sem("exp_neg_set")
        route, inverted, weight_set = sem("route"), sem("inverted"), sem("weight_set")
        log_set, guess_set, root_set = sem("log_set"), sem("guess_set"), sem("root_set")
        root_spread = sem("root_spread")
        rootT_made, rootT_kept = sem("rootT_made"), sem("rootT_kept")
        relu_set, g_set = sem("relu_set"), sem("g_set")
        h_made, r2_square = sem("h_made"), sem("r2_square")
        r2_hi, r2_lo, down_done = sem("r2_hi"), sem("r2_lo"), sem("down_done")
        z_sum, z_bn = sem("z_sum"), sem("z_bn")
        z_stats, z_scale, z_set = sem("z_stats"), sem("z_scale"), sem("z_set")
        GATE_PARTS, PARTS = 9, 11
        ROUTE = 13

        PRODUCTS = ((HI, HI), (LO, HI), (HI, LO))

        def after(eng, signal, per, k, n):
            count = k * per + n
            if not isinstance(count, int) or count > 0:
                eng.wait_ge(signal, count)

        def after_alone(eng, signal, per, k, n):
            count = k * per + n
            if not isinstance(count, int):
                count = eng.lower_val(count)
            if not isinstance(count, int) or count > 0:
                eng.wait_ge(pool_const, 9)
                eng.wait_ge(signal, count)

        def after_gated(eng, c, b):
            if 0 <= b < SH:
                after(eng, relu_set, SH, c, b + 1)
            elif b >= SH:
                after(eng, g_set, NB - SH, c, b - SH + 1)
            elif b < 0:
                after(eng, g_set, NB - SH, c, b + 1)

        def is_step(k, n):
            return isinstance(k, int) and k == n

        def run(eng, step):
            for k in range(4):
                step(k, k % 4, k // 2, "ABCD"[:k + 1])
            with eng.Fori(1, SEQ // 4) as turn:
                for n in range(4):
                    step(turn * 4 + n, n, turn * 2 + n // 2, "ABCD")
            for n, k in enumerate(range(SEQ, SEQ + 3)):
                step(k, k % 4, k // 2, "ABCD"[n + 1:])

        block = ctx.enter_context(nc.Block())

        @block.sync
        def _(sp):
            sp.dma_start(wq_sb[:], Wq).then_inc(scores_in, 16)
            sp.dma_start(wk_sb[:], Wk).then_inc(scores_in, 16)
            sp.dma_start(bk_sb[:], column(bk)).then_inc(scores_in, 16)
            sp.dma_start(bq_sb[:], column(bq)).then_inc(scores_in, 16)
            sp.dma_start(xT[0][:], XT[0]).then_inc(xT_in[0], 16)
            sp.dma_start(wvr[:, 0:E], WvT).then_inc(values_in, 16)
            sp.dma_start(bvr[:, 0:E], row(bv).to_broadcast([P, E])).then_inc(values_in, 16)
            sp.dma_start(gate_sb[:], gateT).then_inc(experts_in, 16)
            sp.dma_start(up_sb[:], up).then_inc(experts_in, 16)
            sp.dma_start(down_sb[:], down).then_inc(experts_in, 16)
            sp.dma_start(gbias[:], row(gate_bias).to_broadcast([P, NX])).then_inc(experts_in, 16)
            sp.dma_start(xT[1][:], XT[1]).then_inc(xT_in[1], 16)
            sp.dma_start(x_sb[0][:], tokens(X, 0)).then_inc(x_in[0], 16)
            sp.dma_start(x_sb[1][:], tokens(X, 1)).then_inc(x_in[1], 16)

            def load(k, par):
                after(sp, s_made, NT, k - 2, NT)
                after(sp, v_made, 2, k - 2, 2)
                sp.dma_start(xT[par][:], XT[bass.ds(k, 1)].rearrange("a p t -> (a p) t")).then_inc(xT_in[par], 16)
                after(sp, y_set, 1, k - 2, 1)
                sp.dma_start(x_sb[par][:], tokens(X, k)).then_inc(x_in[par], 16)

            def store(k, par):
                after(sp, z_set, 1, k, 1)
                sp.dma_start(tokens(out, k), z_out[par][:]).then_inc(stored[par], 16)

            def step(k, par, loads=True, stores=True):
                if stores:
                    store(k - 3, 1 - par)
                if loads:
                    load(k + 2, par)

            for k in range(4):
                step(k, k % 2, stores=k >= 3)
            with sp.Fori(2, SEQ // 2 - 1) as turn:
                step(turn * 2, 0)
                step(turn * 2 + 1, 1)
            for k in range(SEQ - 2, SEQ + 3):
                step(k, k % 2, loads=False)
            for par in range(2):
                sp.wait_ge(stored[par], 16 * (SEQ // 2 + 1))

        @block.gpsimd
        def _(pool):
            pool.memset(ident[:], 0.0).then_inc(pool_const, 1)
            pool.memset(mask16[:], 0.0).then_inc(pool_const, 1)
            pool.memset(tie[:], SMALLEST).then_inc(pool_const, 1)
            pool.memset(minus_half[:], -0.5)
            pool.memset(z_out[0][:, 0, 0:1], 0.0).then_inc(stored[0], 16)
            pool.memset(z_out[1][:, 0, 0:1], 0.0).then_inc(stored[1], 16)
            pool.memset(eps_ln[:], EPS_LN).then_inc(pool_const, 1)
            pool.wait_ge(pool_const, 4)
            pool.affine_select(out=ident[:], in_=ident[:], compare_op=ALU.not_equal, fill=1.0, base=0,
                               pattern=[[-1, P]], channel_multiplier=1).then_inc(pool_const, 1)
            pool.affine_select(out=mask16[:], in_=mask16[:], compare_op=ALU.is_ge, fill=MASKED, base=0,
                               pattern=[[1, P]], channel_multiplier=-1).then_inc(pool_const, 1)
            pool.affine_select(out=tie[:], in_=tie[:], compare_op=ALU.is_ge, fill=0.0, base=0,
                               pattern=[[-1, NX], [1, NX]], channel_multiplier=0).then_inc(pool_const, 1)
            pool.wait_ge(pool_const, 7)
            pool.tensor_copy(ident_half[:], ident[:]).then_inc(pool_const, 1)
            pool.tensor_copy(ident16[:], ident[:]).then_inc(pool_const, 1)

            pool.wait_ge(largest_set, 1)
            pool.partition_all_reduce(largest_all[:], largest[:], P, RMAX).then_inc(largest_set, 1)

            def low_part(c, b):
                after(pool, r2_hi, NB, c, b + 1)
                pool.tensor_tensor(r2[b % 3][:, LO], r2_sb[b % 2][:], r2[b % 3][:, HI], ALU.subtract).then_inc(r2_lo, 1)

            def rank_differences(m):
                after(pool, route, ROUTE, m, 7)
                pool.tensor_tensor(diff[:], masked[:].unsqueeze(2).to_broadcast([P, NT, NX, NX]),
                                   masked[:].unsqueeze(3).to_broadcast([P, NT, NX, NX]), ALU.subtract).then_inc(route, 1)

            def routing_weight(m):
                after(pool, inverted, 1, m, 1)
                after(pool, root_set, 4, m, -3)
                pool.tensor_tensor(weight[:], chosen[:], weight_inv[:].unsqueeze(2).to_broadcast([P, NT, NX]), ALU.mult)\
                    .then_inc(weight_set, 1)

            def root_of_weight(c):
                after(pool, guess_set, 1, c, 1)
                after(pool, root_spread, 1, c, 0)
                pool.tensor_tensor(guess_weight[:], root_guess[:], weight[:], ALU.mult).then_inc(root_set, 1)
                after(pool, root_set, 4, c, 1)
                pool.tensor_tensor(guess2[:], guess_weight[:], root_guess[:], ALU.mult).then_inc(root_set, 1)
                after_alone(pool, root_set, 4, c, 2)
                pool.tensor_scalar(newton[:], guess2[:], -0.5, 1.5, ALU.mult, ALU.add).then_inc(root_set, 1)
                after(pool, root_set, 4, c, 3)
                pool.tensor_tensor(root[:], newton[:], guess_weight[:], ALU.mult).then_inc(root_set, 1)

            def token_scale(k, n, scale_set, per):
                pool.tensor_tensor(var_eps[n][:], mean_var[n][:, :, 1], eps_ln[:], ALU.add).then_inc(scale_set, 1)
                after(pool, scale_set, per, k, 1)
                pool.tensor_tensor(rstd[n][:], var_eps[n][:], minus_half[:], ALU.pow).then_inc(scale_set, 1)

            def step(k, turn4, half_k, stages):
                A, B, C, D = (x in stages for x in "ABCD")
                m, c, d, par = k - 1, k - 2, k - 3, turn4 % 2

                if B:
                    after(pool, y_stats, 1, m, 1)
                    after(pool, x1_set, 1, m, 0)
                    token_scale(m, 0, y_scale, 2)
                if C:
                    routing_weight(c)
                    root_of_weight(c)
                    low_part(c, 0)
                if B:
                    after(pool, x1_hi, 1, m, 1)
                    pool.tensor_tensor(x1_parts[:, LO], x1[(turn4 - 1) % 4][:], x1_parts[:, HI], ALU.subtract).then_inc(x1_lo, 1)
                if C:
                    low_part(c, 1)
                    low_part(c, 2)
                if A:
                    after(pool, inv_set, 1, k, 1)
                    after(pool, v_kept, 2, k, 2)
                    after(pool, o_made, 1, k, 0)
                    pool.tensor_tensor(vn[:], v_sb[:, :, 0:E], prob_inv[:].unsqueeze(2).to_broadcast([P, NT, E]), ALU.mult)\
                        .then_inc(v_scaled, 1)
                if D:
                    after(pool, z_stats, 1, d, 1)
                    after(pool, z_set, 1, d, 0)
                    token_scale(d, 1, z_scale, 2)
                if C:
                    low_part(c, 3)
                    low_part(c, 4)
                if B:
                    rank_differences(m)
                if C:
                    low_part(c, 5)
            run(pool, step)

        @block.scalar
        def _(act):
            act.preload_act_table_set("natural_log_exp_and_others")
            act.wait_ge(setup_made, 1)
            act.mul(m_sb[:], bank_a[:, 0:E], SCALE)
            act.mul(c_sb[:], bank_a[:, E:E + 1], SCALE)
            act.mul(wvr[:, E:E + 1], bank_a[:, E + 1:E + 2], SCALE)
            act.mul(bvr[:, E:E + 1], bank_a[:, E + 2:E + 3], SCALE).then_inc(setup_kept, 1)
            act.wait_ge(setup_kept, 1)

            def high_parts():
                act.wait_ge(parts_set, GATE_PARTS)
                act.mul(up_parts[:, HI], up_sb[:], over2[:, 1:2]).then_inc(parts_hi, 1)
                act.mul(down_parts[:, HI], down_sb[:], over2[:, 2:3]).then_inc(parts_hi, 1)

            def exponentials(k, j):
                n = T - P * j
                after(act, shift_set, NT, k, j + 1)
                after(act, o_made, 1, k, 0)
                act.activation(probsT[:, S_AT[j]:S_AT[j] + n], bank_s[j % 2][:, 0:n], ACT.Exp,
                               bias=shift[:, j:j + 1], accum_out=prob_sum[:, j:j + 1]).then_inc(exp_done, 1)

            def shared_relu(c, b):
                after(act, h_made, NB, c, b + 1)
                after(act, r2_hi, NB, c, b - 1)
                act.activation(g_sb[b % 2][:], bank_h[b % 2][:], ACT.Relu).then_inc(relu_set, 1)

            def square(c, b):
                after_gated(act, c, b)
                after(act, r2_lo, NB, c, b - 1)
                after(act, down_done, NB, c, b - 2)
                act.activation(r2_sb[b % 2][:], g_sb[b % 2][:], ACT.Square).then_inc(r2_square, 1)
                act.activation(r2[b % 3][:, HI], g_sb[b % 2][:], ACT.Square).then_inc(r2_hi, 1)

            def step(k, turn4, half_k, stages):
                A, B, C, D = (x in stages for x in "ABCD")
                m, c, d, par = k - 1, k - 2, k - 3, turn4 % 2
                

                if D:
                    square(d, 4)
                if A:
                    if is_step(k, 1):
                        high_parts()
                    after(act, w_made, 1, k, 1)
                    act.activation(wT[:], bank_a[:], ACT.Identity, bias=c_sb[:, 0:1]).then_inc(w_kept, 1)
                if D:
                    square(d, 5)
                if C:
                    shared_relu(c, 0)
                    square(c, 0)
                    shared_relu(c, 1)
                if A:
                    exponentials(k, 0)
                if C:
                    after(act, weight_set, 1, c, 1)
                    act.activation(log_weight[:], weight[:], ACT.Ln, bias=weight_floor[:, 0:1]).then_inc(log_set, 1)
                    after(act, log_set, 1, c, 1)
                    after(act, root_set, 4, c, 0)
                    act.activation(root_guess[:], log_weight[:], ACT.Exp, scale=-0.5).then_inc(guess_set, 1)
                if A:
                    exponentials(k, 1)
                if C:
                    square(c, 1)
                    after(act, root_set, 4, c, 4)
                    after(act, rootT_made, 1, c, 0)
                    act.copy(root_wide[:], root[:].rearrange("p t e -> p (t e)").unsqueeze(2)
                             .to_broadcast([P, NT * NX, P // NX])).then_inc(root_spread, 1)
                if B:
                    after(act, x1_set, 1, m, 1)
                    after(act, x1T_made, 1, m, 0)
                    act.copy(x1_parts[:, HI], x1[(turn4 - 1) % 4][:]).then_inc(x1_hi, 1)
                if C:
                    after(act, rootT_made, 1, c, 1)
                    after(act, g_set, NB - SH, c, 0)
                    act.copy(rootT[:], bank_b[:]).then_inc(rootT_kept, 1)
                if A:
                    exponentials(k, 2)
                    exponentials(k, 3)
                if C:
                    square(c, 2)
                if B:
                    after(act, x1T_made, 1, m, 1)
                    after(act, h_made, NB, c, 0)
                    act.copy(x1T[1 - par][:].rearrange("p a t -> p (a t)"), bank_o[:].bitcast(F16)).then_inc(x1T_kept, 1)
                if C:
                    square(c, 3)
                if B:
                    after(act, logits_made, 1, m, 1)
                    after(act, weight_set, 1, m, 0)
                    act.activation(exp_neg[:], bank_b[:, 0:NT * NX].rearrange("p (t e) -> p t e", e=NX), ACT.Exp,
                                   scale=neg_gate_unit[:, 0:1]).then_inc(exp_neg_set, 1)
            run(act, step)

        @block.vector
        def _(dve):
            dve.memset(weight_floor[:], WEIGHT_FLOOR)
            dve.wait_ge(scores_in, 16 * 4)
            dve.tensor_copy(bq_wide[:], bq_sb[:, 0:1].to_broadcast([P, P])).then_inc(bq_spread, 1)
            dve.wait_ge(experts_in, 16 * 4)
            for n, w in enumerate((gate_sb, up_sb, down_sb)):
                flat = w[:] if n == 0 else w[:].rearrange("p b c -> p (b c)")
                last = dve.tensor_reduce(largest[:, n:n + 1], flat, AX.X, ALU.max, apply_absolute_value=True)
            last.then_inc(largest_set, 1)
            dve.wait_ge(setup_kept, 1)
            dve.wait_ge(values_in, 16 * 2)
            dve.wait_ge(pool_const, 9)
            parts = [0]

            def prepared(instruction):
                parts[0] += 1
                instruction.then_inc(parts_set, 1)
                dve.wait_ge(parts_set, parts[0])

            def low_of(n, w, halves):
                prepared(dve.scalar_tensor_tensor(out=halves[:, LO], in0=w[:], scalar=over2[:, n:n + 1], in1=halves[:, HI],
                                                  op0=ALU.mult, op1=ALU.subtract))

            def split_gate():
                dve.wait_ge(largest_set, 2)
                prepared(dve.tensor_scalar(largest[:], largest_all[:], UNIT_FLOOR, None, ALU.max))
                prepared(dve.tensor_scalar(floor2[:].bitcast(I32), largest[:].bitcast(I32), EXPONENT_BITS, None, ALU.bitwise_and))
                prepared(dve.reciprocal(over2[:], floor2[:]))
                prepared(dve.tensor_scalar(over2[:], over2[:], 0.5, None, ALU.mult))
                prepared(dve.tensor_scalar(neg_gate_unit[:], floor2[:, 0:1], -2.0, None, ALU.mult))
                prepared(dve.tensor_tensor(up_unit2[:], floor2[:, 1:2], floor2[:, 1:2], ALU.mult))
                prepared(dve.scalar_tensor_tensor(out=ffn_unit[:], in0=up_unit2[:], scalar=8.0, in1=floor2[:, 2:3],
                                                  op0=ALU.mult, op1=ALU.mult))
                prepared(dve.tensor_scalar(gate_parts[:, HI], gate_sb[:], over2[:, 0:1], None, ALU.mult))
                low_of(0, gate_sb, gate_parts)
                assert parts[0] == GATE_PARTS

            def split_experts():
                dve.wait_ge(parts_hi, 2)
                low_of(1, up_sb, up_parts)
                low_of(2, down_sb, down_parts)
                assert parts[0] == PARTS

            fours = biased[:].rearrange("p t (g i) -> p (t g) i", i=GROUP)
            fours_mask = group_mask[:].rearrange("p t g -> p (t g)").unsqueeze(2).to_broadcast([P, 2 * NT, GROUP])

            def route_link(m, n):
                after(dve, route, ROUTE, m, n)
                if n == 0:
                    after(dve, exp_neg_set, 1, m, 1)
                    last = dve.tensor_scalar(one_plus[:], exp_neg[:], 1.0, None, ALU.add)
                elif n == 1:
                    last = dve.reciprocal(score[:], one_plus[:])
                elif n == 2:
                    last = dve.tensor_tensor(biased[:], score[:], gbias[:].unsqueeze(1).to_broadcast([P, NT, NX]), ALU.add)
                elif n == 3:
                    dve.tensor_tensor(pair_sum[:, :, 0:3], fours[:, :, 0:3], fours[:, :, 1:4], ALU.add)
                    dve.tensor_tensor(pair_sum[:, :, 3:5], fours[:, :, 0:2], fours[:, :, 2:4], ALU.add)
                    last = dve.tensor_tensor(pair_sum[:, :, 5], fours[:, :, 0], fours[:, :, 3], ALU.add)
                elif n == 4:
                    last = dve.tensor_reduce(group_score[:].rearrange("p t g -> p (t g)"), pair_sum[:], AX.X, ALU.max)
                elif n == 5:
                    dve.tensor_tensor(group_mask[:, :, 0], group_score[:, :, 0], group_score[:, :, 1], ALU.is_ge)
                    last = dve.tensor_tensor(group_mask[:, :, 1], group_score[:, :, 0], group_score[:, :, 1], ALU.is_lt)
                elif n == 6:
                    last = dve.tensor_tensor(masked[:].rearrange("p t (g i) -> p (t g) i", i=GROUP), fours, fours_mask, ALU.mult)
                elif n == 8:
                    last = dve.tensor_tensor(ahead[:].rearrange("p t e j -> p t (e j)"), diff[:].rearrange("p t e j -> p t (e j)"),
                                             tie[:].rearrange("p e j -> p (e j)").unsqueeze(1).to_broadcast([P, NT, NX * NX]),
                                             ALU.is_ge)
                elif n == 9:
                    last = dve.tensor_reduce(rank[:], ahead[:], AX.X, ALU.add)
                elif n == 10:
                    last = dve.scalar_tensor_tensor(out=chosen[:], in0=rank[:], scalar=2.0, in1=score[:], op0=ALU.is_lt,
                                                    op1=ALU.mult)
                elif n == 11:
                    last = dve.tensor_reduce(weight_sum[:], chosen[:], AX.X, ALU.add)
                elif n == 12:
                    last = dve.tensor_scalar(weight_den[:], weight_sum[:], EPS_TOPK, 1.0 / ROUTED_SCALE, ALU.add, ALU.mult)
                last.then_inc(route, 1)

            def route_end(m):
                after(dve, route, ROUTE, m, ROUTE)
                after(dve, weight_set, 1, m, 0)
                dve.reciprocal(weight_inv[:], weight_den[:]).then_inc(inverted, 1)

            def gated(c, b):
                after(dve, h_made, NB, c, b + 1)
                after(dve, r2_hi, NB, c, b - 1)
                after(dve, rootT_kept, 1, c, 1)
                dve.scalar_tensor_tensor(out=g_sb[b % 2][:], in0=bank_h[b % 2][:], scalar=0.0, in1=rootT[:],
                                         op0=ALU.max, op1=ALU.mult).then_inc(g_set, 1)

            def values(k, n, bank):
                after(dve, v_made, 2, k, n + 1)
                after(dve, v_scaled, 1, k, 0)
                dve.tensor_tensor(v_sb[:, 2 * n:2 * n + 2, :], bank[:, 0:2 * (E + 1)].rearrange("p (t e) -> p t e", t=2),
                                  bvr[:].unsqueeze(1).to_broadcast([P, 2, E + 1]), ALU.add).then_inc(v_kept, 1)

            def key_max(k, j):
                after(dve, s_made, NT, k, j + 1)
                dve.reduce_max(neg_max[:, j:j + 1], bank_s[j % 2][:, 0:T - P * j], AX.X, negate=True).then_inc(max_set, 1)

            def key_shift(k, j):
                after(dve, max_set, NT, k, j + 1)
                after(dve, v_kept, 2, k, j // 2 + 1)
                dve.tensor_scalar(shift[:, j:j + 1], neg_max[:, j:j + 1], v_sb[:, j, E:E + 1], v_sb[:, j, E:E + 1],
                                  ALU.subtract, ALU.add).then_inc(shift_set, 1)

            def token_sums(seq, src, n, summed, bn):
                after(dve, summed, 1, seq, 1)
                for t in range(NT):
                    last = dve.bn_stats(stats[n][:, t, :], src[:, t, :])
                last.then_inc(bn, 1)

            def token_stats(seq, n, bn, done):
                after_alone(dve, bn, 1, seq, 1)
                for t in range(NT):
                    last = dve.bn_aggr(mean_var[n][:, t, :], stats[n][:, t, :])
                last.then_inc(done, 1)

            def normalise(seq, src, n, dst, scale_set, done):
                after(dve, z_sum, 1, seq, -2)
                after(dve, scale_set, 2, seq, 2)
                for t in range(NT):
                    last = dve.tensor_scalar(dst[:, t, :], src[:, t, :], mean_var[n][:, t, 0:1], rstd[n][:, t:t + 1],
                                             ALU.subtract, ALU.mult)
                last.then_inc(done, 1)

            def step(k, turn4, half_k, stages):
                A, B, C, D = (x in stages for x in "ABCD")
                m, c, d, par = k - 1, k - 2, k - 3, turn4 % 2

                if B:
                    token_sums(m, y_sb, 0, y_set, y_bn)
                if C:
                    route_link(c, 8)
                if B:
                    token_stats(m, 0, y_bn, y_stats)
                if C:
                    route_link(c, 9)
                if A:
                    values(k, 0, bank_a)
                if C:
                    route_link(c, 10)
                if A:
                    key_max(k, 0)
                if C:
                    route_link(c, 11)
                if A:
                    key_shift(k, 0)
                if C:
                    route_link(c, 12)
                    route_end(c)
                if A:
                    key_max(k, 1)
                    key_shift(k, 1)
                if B:
                    normalise(m, y_sb, 0, x1[(turn4 - 1) % 4], y_scale, x1_set)
                if A:
                    values(k, 1, bank_b)
                if D:
                    after(dve, down_done, NB, d, NB)
                    after(dve, z_set, 1, d, 0)
                    dve.scalar_tensor_tensor(out=z_sb[:].rearrange("p t e -> p (t e)"), in0=bank_y[:], scalar=ffn_unit[:, 0:1],
                                             in1=x1[(turn4 - 3) % 4][:].rearrange("p t e -> p (t e)"), op0=ALU.mult, op1=ALU.add).then_inc(z_sum, 1)
                if A:
                    key_max(k, 2)
                    key_max(k, 3)
                    key_shift(k, 2)
                    key_shift(k, 3)
                if C:
                    gated(c, 2)
                if A:
                    after(dve, exp_done, NT, k, NT)
                    dve.reciprocal(prob_inv[:], prob_sum[:]).then_inc(inv_set, 1)
                    if is_step(k, 0):
                        split_gate()
                    if is_step(k, 1):
                        split_experts()
                if C:
                    gated(c, 3)
                if D:
                    token_sums(d, z_sb, 1, z_sum, z_bn)
                    token_stats(d, 1, z_bn, z_stats)
                if C:
                    gated(c, 4)
                    gated(c, 5)
                if B:
                    route_link(m, 0)
                    route_link(m, 1)
                    route_link(m, 2)
                    route_link(m, 3)
                    route_link(m, 4)
                    route_link(m, 5)
                if D:
                    after(dve, z_scale, 2, d, 2)
                    after(dve, stored[1 - par], 16, half_k - 2 + par, 16)
                    for t in range(NT):
                        last = dve.tensor_scalar(z_out[1 - par][:, t, :], z_sb[:, t, :], mean_var[1][:, t, 0:1], rstd[1][:, t:t + 1],
                                                 ALU.subtract, ALU.mult)
                    last.then_inc(z_set, 1)
                if B:
                    route_link(m, 6)
                if A:
                    after(dve, o_made, 1, k, 1)
                    after(dve, x_in[par], 16, half_k, 16)
                    after(dve, x1_set, 1, k, 0)
                    dve.tensor_tensor(y_sb[:].rearrange("p t e -> p (t e)"), bank_o[:],
                                      x_sb[par][:].rearrange("p t e -> p (t e)"), ALU.add).then_inc(y_set, 1)
            run(dve, step)

        @block.tensor
        def _(pe):
            pe.wait_ge(scores_in, 16 * 4)
            pe.wait_ge(bq_spread, 1)
            pe.matmul(bank_a[:, 0:E], wk_sb[:], wq_sb[:], start=True, stop=True)
            pe.matmul(bank_a[:, E:E + 1], wq_sb[:], bk_sb[:], start=True, stop=True)
            pe.matmul(bank_a[:, E + 1:E + 2], wk_sb[:], bq_sb[:], start=True, stop=True)
            pe.matmul(bank_a[:, E + 2:E + 3], bq_wide[:], bk_sb[:], start=True, stop=True).then_inc(setup_made, 1)
            pe.wait_ge(setup_kept, 1)
            pe.wait_ge(values_in, 16 * 2)
            pe.wait_ge(pool_const, 9)

            def up_block(c, par, b):
                after_gated(pe, c, b - 2)
                for n, (w, x) in enumerate(PRODUCTS):
                    last = pe.matmul(bank_h[b % 2][:], up_parts[:, w, b], x1T[par][:, x], start=(n == 0), stop=(n == 2))
                last.then_inc(h_made, 1)

            def down_block(c, b):
                after(pe, r2_lo, NB, c, b + 1)
                if b == 0:
                    after(pe, z_sum, 1, c, 0)
                for t in range(NT):
                    for n, (w, r) in enumerate(PRODUCTS):
                        last = pe.matmul(bank_y[:, t * E:(t + 1) * E], r2[b % 3][:, r, t * P:(t + 1) * P],
                                         down_parts[:, w, b], start=(b == 0 and t == 0 and n == 0),
                                         stop=(b == NB - 1 and n == 2), skip_group_check=True)
                last.then_inc(down_done, 1)

            def values(k, par, n, bank):
                for t in range(2):
                    tile = 2 * n + t
                    last = pe.matmul(bank[:, t * (E + 1):(t + 1) * (E + 1)], xT[par][:, tile * P:(tile + 1) * P], wvr[:],
                                     start=True, stop=True)
                last.then_inc(v_made, 1)

            def scores(k, par, j):
                n = T - P * j
                after(pe, w_kept, 1, k, 1)
                after(pe, exp_done, NT, k, j - 1)
                pe.matmul(bank_s[j % 2][:, 0:n], wT[:, j * P:(j + 1) * P], xT[par][:, j * P:T], start=True, stop=False,
                          skip_group_check=True)
                pe.matmul(bank_s[j % 2][:, 0:P], ident16[:], mask16[:], start=False, stop=True,
                          skip_group_check=True).then_inc(s_made, 1)

            def step(k, turn4, half_k, stages):
                A, B, C, D = (x in stages for x in "ABCD")
                m, c, d, par = k - 1, k - 2, k - 3, turn4 % 2

                if A:
                    after(pe, xT_in[par], 16, half_k, 16)
                    after(pe, v_kept, 2, k, -1)
                    pe.matmul(bank_a[:], m_sb[:], xT[par][:], start=True, stop=True).then_inc(w_made, 1)
                if B:
                    after(pe, v_scaled, 1, m, 1)
                    after(pe, exp_done, NT, m, NT)
                    after(pe, x1T_kept, 1, m, 0)
                    for t in range(NT):
                        for j in range(t + 1):
                            at = S_AT[j] + (t - j) * P
                            last = pe.matmul(bank_o[:, t * E:(t + 1) * E], probsT[:, at:at + P], vn[:, j, :],
                                             start=(j == 0), stop=(j == t))
                    last.then_inc(o_made, 1)
                if C:
                    if is_step(k, 2):
                        pe.wait_ge(parts_set, PARTS)
                    up_block(c, par, 0)
                if A:
                    after(pe, w_kept, 1, k, 1)
                    values(k, par, 0, bank_a)
                if D:
                    down_block(d, 3)
                if A:
                    scores(k, par, 0)
                if C:
                    up_block(c, par, 1)
                if A:
                    scores(k, par, 1)
                if D:
                    down_block(d, 4)
                if A:
                    after(pe, exp_neg_set, 1, k, -1)
                    values(k, par, 1, bank_b)
                if D:
                    down_block(d, 5)
                if C:
                    up_block(c, par, 2)
                if A:
                    scores(k, par, 2)
                if C:
                    up_block(c, par, 3)
                if A:
                    scores(k, par, 3)
                if C:
                    after(pe, root_spread, 1, c, 1)
                    if A:
                        after(pe, v_kept, 2, k, 2)
                    for t in range(NT):
                        last = pe.transpose(bank_b[:, t * P:(t + 1) * P],
                                            root_wide[:, t * NX:(t + 1) * NX].rearrange("p e c -> p (e c)"), ident[:])
                    last.then_inc(rootT_made, 1)
                    down_block(c, 0)
                if B:
                    after(pe, x1_lo, 1, m, 1)
                    after(pe, y_set, 1, m, 1)
                    for x in (HI, LO):
                        for t in range(NT):
                            at = x * T + t * P
                            last = pe.transpose(bank_o[:].bitcast(F16)[:, at:at + P], x1_parts[:, x, t, :], ident_half[:])
                    last.then_inc(x1T_made, 1)
                if C:
                    up_block(c, par, 4)
                    down_block(c, 1)
                    up_block(c, par, 5)
                if B:
                    if is_step(k, 1):
                        pe.wait_ge(parts_set, GATE_PARTS)
                    after(pe, rootT_kept, 1, c, 1)
                    if is_step(k, 1):
                        after(pe, v_kept, 2, k, 2)
                    after(pe, x1T_kept, 1, m, 1)
                    for t in range(NT):
                        for n, (w, x) in enumerate(PRODUCTS):
                            last = pe.matmul(bank_b[:, t * NX:(t + 1) * NX], x1T[1 - par][:, x, t * P:(t + 1) * P],
                                             gate_parts[:, w], start=(n == 0), stop=(n == 2))
                    last.then_inc(logits_made, 1)
                if C:
                    down_block(c, 2)
            run(pe, step)


def kernel(**inputs):
    import numpy as np
    import concourse.bacc as bacc
    from concourse.bass_utils import run_bass_kernel_spmd

    a = {name: np.asarray(value) for name, value in inputs.items()}
    X = a["L0_attn_X"]
    seq, t, e = X.shape
    routed_up, routed_down = a["L0_ffn_up_weights"], a["L0_ffn_down_weights"]
    nx, width, h = routed_up.shape
    share = P // nx
    shared_up, shared_down = a["L0_ffn_shared_up_weight"], a["L0_ffn_shared_down_weight"]
    up = np.concatenate([
        shared_up.reshape(-1, P, h).transpose(2, 0, 1),
        routed_up.reshape(nx, width // share, share, h).transpose(3, 1, 0, 2).reshape(h, width // share, P)], 1)
    down = np.concatenate([
        shared_down.reshape(h, -1, P).transpose(2, 1, 0),
        routed_down.reshape(nx, h, width // share, share).transpose(0, 3, 2, 1).reshape(P, width // share, h)], 1)
    arrays = {
        "X": X, "XT": X.transpose(0, 2, 1), "Wq": a["L0_attn_Wq"], "Wk": a["L0_attn_Wk"], "WvT": a["L0_attn_Wv"].T,
        "bq": a["L0_attn_bq"], "bk": a["L0_attn_bk"], "bv": a["L0_attn_bv"], "gateT": a["L0_ffn_gate_weight"].T,
        "gate_bias": a["L0_ffn_gate_bias"], "up": up, "down": down,
    }
    arrays = {name: np.ascontiguousarray(value) for name, value in arrays.items()}
    nc = bacc.Bacc("TRN2", target_bir_lowering=False, num_devices=1)
    args = {name: nc.dram_tensor(name, value.shape, F32, kind="ExternalInput").ap() for name, value in arrays.items()}
    args["out"] = nc.dram_tensor("out", X.shape, F32, kind="ExternalOutput").ap()
    layer_program(nc, **args)
    return run_bass_kernel_spmd(nc, [arrays], core_ids=[0]).results[0]["out"]
```
